# Optimizing a Trainium2 kernel written in Bass

```python
import numpy as np
import jax
import jax.numpy as jnp

def _softmax(x, axis=-1):
    return jax.nn.softmax(x, axis=axis)

def _gelu(x):
    return jax.nn.gelu(x, approximate=True)

def _silu(x):
    return jax.nn.silu(x)

def _sigmoid(x):
    return jax.nn.sigmoid(x)

def _layernorm(x, axis=-1, eps=1e-05):
    m = jnp.mean(x, axis=axis, keepdims=True)
    v = jnp.var(x, axis=axis, keepdims=True)
    return (x - m) / jnp.sqrt(v + eps)

def _scatter_add(tgt, idx, src, axis=0):
    return tgt.at[idx].add(src)

def _segment_sum(src, seg, n):
    return jax.ops.segment_sum(src, seg, n)
kernel_name = 'mk_dlrm_tower_d1_rec_r8_db6373'

def setup_inputs(seed: int=0):
    np.random.seed(seed)
    _w = jnp.asarray

    def _rec_inputs():
        import jax
        import jax.numpy as jnp
        _tk = jax.random.key(seed)
        dense_ctx = jax.random.normal(jax.random.fold_in(_tk, 190), (2048, 16), jnp.float32)
        ids = jnp.stack([jax.random.randint(jax.random.fold_in(_tk, 200 + f), (2048,), 0, v, jnp.int32) for f, v in enumerate([1000, 12500, 1250, 1250, 12500, 125000, 125000, 125000, 12500, 1250, 1000, 12500, 12500, 12500, 125000, 125000, 1250, 125000, 12500, 12500, 12500, 12500, 1250, 1250, 1000, 12500, 12500, 1250, 1250, 12500, 1000, 12500, 12500, 12500, 1000, 12500, 1250, 1250, 1000, 1000])], axis=1)
        tbl_0 = 0.05 * jax.random.normal(jax.random.fold_in(_tk, 500 + 0), (1000, 32), jnp.float32)
        tbl_1 = 0.05 * jax.random.normal(jax.random.fold_in(_tk, 500 + 1), (12500, 32), jnp.float32)
        tbl_2 = 0.05 * jax.random.normal(jax.random.fold_in(_tk, 500 + 2), (1250, 32), jnp.float32)
        tbl_3 = 0.05 * jax.random.normal(jax.random.fold_in(_tk, 500 + 3), (1250, 32), jnp.float32)
        tbl_4 = 0.05 * jax.random.normal(jax.random.fold_in(_tk, 500 + 4), (12500, 32), jnp.float32)
        tbl_5 = 0.05 * jax.random.normal(jax.random.fold_in(_tk, 500 + 5), (125000, 32), jnp.float32)
        tbl_6 = 0.05 * jax.random.normal(jax.random.fold_in(_tk, 500 + 6), (125000, 32), jnp.float32)
        tbl_7 = 0.05 * jax.random.normal(jax.random.fold_in(_tk, 500 + 7), (125000, 32), jnp.float32)
        tbl_8 = 0.05 * jax.random.normal(jax.random.fold_in(_tk, 500 + 8), (12500, 32), jnp.float32)
        tbl_9 = 0.05 * jax.random.normal(jax.random.fold_in(_tk, 500 + 9), (1250, 32), jnp.float32)
        tbl_10 = 0.05 * jax.random.normal(jax.random.fold_in(_tk, 500 + 10), (1000, 32), jnp.float32)
        tbl_11 = 0.05 * jax.random.normal(jax.random.fold_in(_tk, 500 + 11), (12500, 32), jnp.float32)
        tbl_12 = 0.05 * jax.random.normal(jax.random.fold_in(_tk, 500 + 12), (12500, 32), jnp.float32)
        tbl_13 = 0.05 * jax.random.normal(jax.random.fold_in(_tk, 500 + 13), (12500, 32), jnp.float32)
        tbl_14 = 0.05 * jax.random.normal(jax.random.fold_in(_tk, 500 + 14), (125000, 32), jnp.float32)
        tbl_15 = 0.05 * jax.random.normal(jax.random.fold_in(_tk, 500 + 15), (125000, 32), jnp.float32)
        tbl_16 = 0.05 * jax.random.normal(jax.random.fold_in(_tk, 500 + 16), (1250, 32), jnp.float32)
        tbl_17 = 0.05 * jax.random.normal(jax.random.fold_in(_tk, 500 + 17), (125000, 32), jnp.float32)
        tbl_18 = 0.05 * jax.random.normal(jax.random.fold_in(_tk, 500 + 18), (12500, 32), jnp.float32)
        tbl_19 = 0.05 * jax.random.normal(jax.random.fold_in(_tk, 500 + 19), (12500, 32), jnp.float32)
        tbl_20 = 0.05 * jax.random.normal(jax.random.fold_in(_tk, 500 + 20), (12500, 32), jnp.float32)
        tbl_21 = 0.05 * jax.random.normal(jax.random.fold_in(_tk, 500 + 21), (12500, 32), jnp.float32)
        tbl_22 = 0.05 * jax.random.normal(jax.random.fold_in(_tk, 500 + 22), (1250, 32), jnp.float32)
        tbl_23 = 0.05 * jax.random.normal(jax.random.fold_in(_tk, 500 + 23), (1250, 32), jnp.float32)
        tbl_24 = 0.05 * jax.random.normal(jax.random.fold_in(_tk, 500 + 24), (1000, 32), jnp.float32)
        tbl_25 = 0.05 * jax.random.normal(jax.random.fold_in(_tk, 500 + 25), (12500, 32), jnp.float32)
        tbl_26 = 0.05 * jax.random.normal(jax.random.fold_in(_tk, 500 + 26), (12500, 32), jnp.float32)
        tbl_27 = 0.05 * jax.random.normal(jax.random.fold_in(_tk, 500 + 27), (1250, 32), jnp.float32)
        tbl_28 = 0.05 * jax.random.normal(jax.random.fold_in(_tk, 500 + 28), (1250, 32), jnp.float32)
        tbl_29 = 0.05 * jax.random.normal(jax.random.fold_in(_tk, 500 + 29), (12500, 32), jnp.float32)
        tbl_30 = 0.05 * jax.random.normal(jax.random.fold_in(_tk, 500 + 30), (1000, 32), jnp.float32)
        tbl_31 = 0.05 * jax.random.normal(jax.random.fold_in(_tk, 500 + 31), (12500, 32), jnp.float32)
        tbl_32 = 0.05 * jax.random.normal(jax.random.fold_in(_tk, 500 + 32), (12500, 32), jnp.float32)
        tbl_33 = 0.05 * jax.random.normal(jax.random.fold_in(_tk, 500 + 33), (12500, 32), jnp.float32)
        tbl_34 = 0.05 * jax.random.normal(jax.random.fold_in(_tk, 500 + 34), (1000, 32), jnp.float32)
        tbl_35 = 0.05 * jax.random.normal(jax.random.fold_in(_tk, 500 + 35), (12500, 32), jnp.float32)
        tbl_36 = 0.05 * jax.random.normal(jax.random.fold_in(_tk, 500 + 36), (1250, 32), jnp.float32)
        tbl_37 = 0.05 * jax.random.normal(jax.random.fold_in(_tk, 500 + 37), (1250, 32), jnp.float32)
        tbl_38 = 0.05 * jax.random.normal(jax.random.fold_in(_tk, 500 + 38), (1000, 32), jnp.float32)
        tbl_39 = 0.05 * jax.random.normal(jax.random.fold_in(_tk, 500 + 39), (1000, 32), jnp.float32)
        _rk = jax.random.fold_in(_tk, 7)
        W_top1 = 0.0354441 * jax.random.normal(jax.random.fold_in(_tk, 801), (796, 512), jnp.float32)
        W_top2 = 0.0441942 * jax.random.normal(jax.random.fold_in(_tk, 802), (512, 256), jnp.float32)
        W_top3 = 0.0625 * jax.random.normal(jax.random.fold_in(_tk, 803), (256, 1), jnp.float32)
        b_top1 = jnp.zeros((512,), jnp.float32)
        b_top2 = jnp.zeros((256,), jnp.float32)
        return (dense_ctx, ids, tbl_0, tbl_1, tbl_2, tbl_3, tbl_4, tbl_5, tbl_6, tbl_7, tbl_8, tbl_9, tbl_10, tbl_11, tbl_12, tbl_13, tbl_14, tbl_15, tbl_16, tbl_17, tbl_18, tbl_19, tbl_20, tbl_21, tbl_22, tbl_23, tbl_24, tbl_25, tbl_26, tbl_27, tbl_28, tbl_29, tbl_30, tbl_31, tbl_32, tbl_33, tbl_34, tbl_35, tbl_36, tbl_37, tbl_38, tbl_39, W_top1, b_top1, W_top2, b_top2, W_top3)
    dense_ctx, ids, tbl_0, tbl_1, tbl_2, tbl_3, tbl_4, tbl_5, tbl_6, tbl_7, tbl_8, tbl_9, tbl_10, tbl_11, tbl_12, tbl_13, tbl_14, tbl_15, tbl_16, tbl_17, tbl_18, tbl_19, tbl_20, tbl_21, tbl_22, tbl_23, tbl_24, tbl_25, tbl_26, tbl_27, tbl_28, tbl_29, tbl_30, tbl_31, tbl_32, tbl_33, tbl_34, tbl_35, tbl_36, tbl_37, tbl_38, tbl_39, W_top1, b_top1, W_top2, b_top2, W_top3 = _rec_inputs()

    def _L0_rec_setup():
        import jax, jax.numpy as jnp
        import numpy as np
        NUM_FIELDS = 40
        EMBED_DIM = 32
        BATCH = 512
        NUM_PAIRS = NUM_FIELDS * (NUM_FIELDS - 1) // 2
        key = jax.random.key(seed)
        k1, k2 = jax.random.split(key)
        inputs = jax.random.normal(k1, (BATCH, NUM_FIELDS, EMBED_DIM), dtype=jnp.float32)
        std = (2.0 / (EMBED_DIM + EMBED_DIM)) ** 0.5
        bilinear_matrices = jax.random.normal(k2, (NUM_PAIRS, EMBED_DIM, EMBED_DIM), dtype=jnp.float32) * std
        return {'inputs': inputs, 'bilinear_matrices': bilinear_matrices}
    _L0_rec_all = _L0_rec_setup()
    _L0_rec_in = {k: v for k, v in _L0_rec_all.items() if k in ('bilinear_matrices',)}
    del _L0_rec_all
    return {'dense_ctx': dense_ctx, 'ids': ids, 'tbl_0': tbl_0, 'tbl_1': tbl_1, 'tbl_2': tbl_2, 'tbl_3': tbl_3, 'tbl_4': tbl_4, 'tbl_5': tbl_5, 'tbl_6': tbl_6, 'tbl_7': tbl_7, 'tbl_8': tbl_8, 'tbl_9': tbl_9, 'tbl_10': tbl_10, 'tbl_11': tbl_11, 'tbl_12': tbl_12, 'tbl_13': tbl_13, 'tbl_14': tbl_14, 'tbl_15': tbl_15, 'tbl_16': tbl_16, 'tbl_17': tbl_17, 'tbl_18': tbl_18, 'tbl_19': tbl_19, 'tbl_20': tbl_20, 'tbl_21': tbl_21, 'tbl_22': tbl_22, 'tbl_23': tbl_23, 'tbl_24': tbl_24, 'tbl_25': tbl_25, 'tbl_26': tbl_26, 'tbl_27': tbl_27, 'tbl_28': tbl_28, 'tbl_29': tbl_29, 'tbl_30': tbl_30, 'tbl_31': tbl_31, 'tbl_32': tbl_32, 'tbl_33': tbl_33, 'tbl_34': tbl_34, 'tbl_35': tbl_35, 'tbl_36': tbl_36, 'tbl_37': tbl_37, 'tbl_38': tbl_38, 'tbl_39': tbl_39, 'W_top1': W_top1, 'b_top1': b_top1, 'W_top2': W_top2, 'b_top2': b_top2, 'W_top3': W_top3, 'L0_rec_bilinear_matrices': _L0_rec_in['bilinear_matrices']}

def reference(dense_ctx, ids, tbl_0, tbl_1, tbl_2, tbl_3, tbl_4, tbl_5, tbl_6, tbl_7, tbl_8, tbl_9, tbl_10, tbl_11, tbl_12, tbl_13, tbl_14, tbl_15, tbl_16, tbl_17, tbl_18, tbl_19, tbl_20, tbl_21, tbl_22, tbl_23, tbl_24, tbl_25, tbl_26, tbl_27, tbl_28, tbl_29, tbl_30, tbl_31, tbl_32, tbl_33, tbl_34, tbl_35, tbl_36, tbl_37, tbl_38, tbl_39, W_top1, b_top1, W_top2, b_top2, W_top3, L0_rec_bilinear_matrices):
    import jax
    import jax.numpy as jnp

    def _L0_rec_ref(inputs, bilinear_matrices):
        import jax, jax.numpy as jnp
        import numpy as np
        NUM_FIELDS = 40
        EMBED_DIM = 32
        BATCH = 512
        NUM_PAIRS = NUM_FIELDS * (NUM_FIELDS - 1) // 2
        num_fields = inputs.shape[1]
        iidx, jidx = jnp.triu_indices(num_fields, k=1)
        xi = inputs[:, iidx, :]
        xj = inputs[:, jidx, :]
        out = jnp.einsum('bpd,pde,bpe->bp', xi, bilinear_matrices, xj)
        return out
    e = jnp.stack([tbl_0[ids[:, 0]], tbl_1[ids[:, 1]], tbl_2[ids[:, 2]], tbl_3[ids[:, 3]], tbl_4[ids[:, 4]], tbl_5[ids[:, 5]], tbl_6[ids[:, 6]], tbl_7[ids[:, 7]], tbl_8[ids[:, 8]], tbl_9[ids[:, 9]], tbl_10[ids[:, 10]], tbl_11[ids[:, 11]], tbl_12[ids[:, 12]], tbl_13[ids[:, 13]], tbl_14[ids[:, 14]], tbl_15[ids[:, 15]], tbl_16[ids[:, 16]], tbl_17[ids[:, 17]], tbl_18[ids[:, 18]], tbl_19[ids[:, 19]], tbl_20[ids[:, 20]], tbl_21[ids[:, 21]], tbl_22[ids[:, 22]], tbl_23[ids[:, 23]], tbl_24[ids[:, 24]], tbl_25[ids[:, 25]], tbl_26[ids[:, 26]], tbl_27[ids[:, 27]], tbl_28[ids[:, 28]], tbl_29[ids[:, 29]], tbl_30[ids[:, 30]], tbl_31[ids[:, 31]], tbl_32[ids[:, 32]], tbl_33[ids[:, 33]], tbl_34[ids[:, 34]], tbl_35[ids[:, 35]], tbl_36[ids[:, 36]], tbl_37[ids[:, 37]], tbl_38[ids[:, 38]], tbl_39[ids[:, 39]]], axis=1)
    z = _L0_rec_ref(e, L0_rec_bilinear_matrices)
    z = z.reshape(z.shape[0], -1)
    h = jnp.concatenate([z, dense_ctx], axis=1)
    h = jnp.maximum(h @ W_top1 + b_top1, 0.0)
    h = jnp.maximum(h @ W_top2 + b_top2, 0.0)
    y = h @ W_top3
    return y

_drawn_inputs = setup_inputs


def setup_inputs(seed=0):
    import zlib

    import numpy as np

    out = dict(_drawn_inputs(seed))
    spreads = {'b_top1': (0.0, 0.1), 'b_top2': (0.0, 0.1)}
    factors = {'tbl_0': 3.629,
     'tbl_1': 3.32,
     'tbl_2': 3.452,
     'tbl_3': 3.023,
     'tbl_4': 3.279,
     'tbl_5': 3.19,
     'tbl_6': 3.509,
     'tbl_7': 3.327,
     'tbl_8': 3.081,
     'tbl_9': 2.975,
     'tbl_10': 3.212,
     'tbl_11': 3.587,
     'tbl_12': 3.003,
     'tbl_13': 3.224,
     'tbl_14': 3.284,
     'tbl_15': 3.447,
     'tbl_16': 3.212,
     'tbl_17': 3.227,
     'tbl_18': 3.57,
     'tbl_19': 3.265,
     'tbl_20': 3.078,
     'tbl_21': 3.327,
     'tbl_22': 3.225,
     'tbl_23': 2.947,
     'tbl_24': 3.389,
     'tbl_25': 3.482,
     'tbl_26': 3.159,
     'tbl_27': 3.455,
     'tbl_28': 3.283,
     'tbl_29': 3.203,
     'tbl_30': 3.255,
     'tbl_31': 3.001,
     'tbl_32': 3.357,
     'tbl_33': 3.225,
     'tbl_34': 3.27,
     'tbl_35': 3.161,
     'tbl_36': 3.48,
     'tbl_37': 3.331,
     'tbl_38': 3.479,
     'tbl_39': 3.096}
    for name, (base, spread) in spreads.items():
        noise = np.random.default_rng([zlib.crc32(name.encode()), seed]).standard_normal(out[name].shape)
        drawn = base * np.exp(spread * noise) if base else spread * noise
        out[name] = jnp.asarray(drawn.astype(out[name].dtype))
    for name, factor in factors.items():
        out[name] = (out[name] * factor).astype(out[name].dtype)
    return out
```

```python
import numpy as np
import concourse.bass as bass
import concourse.mybir as mybir
from contextlib import ExitStack

F32 = mybir.dt.float32
F32R = mybir.dt.float32r
I32 = mybir.dt.int32
ALU = mybir.AluOpType
ACT = mybir.ActivationFunctionType

P = 128
FIELDS, DIM = 40, 32
BATCH, DENSE = 2048, 16
H1, H2 = 512, 256
NB = 256
BLOCKS = BATCH // NB
SUB = NB // P
CF = P // DIM
CHUNKS = FIELDS // CF
PAIRS = FIELDS * (FIELDS - 1) // 2

CHUNK_OF_STEP = [CHUNKS - 1 - c for c in range(CHUNKS)]
UNITS = [(a, J) for a in CHUNK_OF_STEP for J in range(CHUNKS - 1, a - 1, -1)]
NU = len(UNITS)
FIRST_UNIT = [UNITS.index((a, CHUNKS - 1)) for a in CHUNK_OF_STEP]
UNITS_OF_STEP = [[k for k in range(NU) if UNITS[k][0] == a] for a in CHUNK_OF_STEP]

UPT = 8
ZT = (NU + UPT - 1) // UPT
DENSE_SLOT = UPT - 1
assert NU % UPT == UPT - 1 and DENSE == CF * CF


def slot_runs():
    runs = []
    for t in range(ZT):
        ks = range(t * UPT, min(NU, (t + 1) * UPT))
        for a in CHUNK_OF_STEP:
            js = [UNITS[k][1] for k in ks if UNITS[k][0] == a]
            if js:
                first = min(k for k in ks if UNITS[k][0] == a) - t * UPT
                runs.append((t, a, min(js), max(js), first))
    return runs


RUNS = slot_runs()
SLOT = {(a, J): slot + J - lo for _, a, lo, hi, slot in RUNS for J in range(lo, hi + 1)}

U_SLOTS, P_SLOTS = 2, 4


def rows_of(k):
    a, J = UNITS[k]
    return range(CF - 1) if a == J else range(CF)


def pair(i, j):
    return i * (FIELDS - 1) - i * (i - 1) // 2 + (j - i - 1)


def before(k, slots):
    n = 1
    while (k - n) % NU % slots != k % slots:
        n += 1
    return n


W_J0 = [CF * (i // CF) + (CF if i % CF == CF - 1 else 0) for i in range(FIELDS)]
W_AT, _n = [0] * FIELDS, 0
for _a in CHUNK_OF_STEP:
    for _i in range(CF * _a, CF * _a + CF):
        W_AT[_i] = _n
        _n += (FIELDS - W_J0[_i]) * DIM
W_COLS = _n
W_REGION = [(W_AT[CF * a], (W_AT[CF * a - CF] if a else W_COLS)) for a in CHUNK_OF_STEP]
PIECE = 1024
W_PIECES, _n = [], 0
for _lo, _hi in W_REGION:
    _xs = range(_lo, _hi, PIECE)
    W_PIECES.append([(_n + m, x, min(x + PIECE, _hi)) for m, x in enumerate(_xs)])
    _n += len(_xs)

W1_LOADS = []
for _t, _a, _lo, _hi, _slot in RUNS:
    for _i in range(CF * _a, CF * _a + CF):
        _j = max(CF * _lo, _i + 1)
        if _j < CF * _hi + CF:
            W1_LOADS.append((_t, DIM * (_i - CF * _a) + CF * _slot + _j - CF * _lo, pair(_i, _j), CF * _hi + CF - _j))
for _r in range(CF):
    W1_LOADS.append((ZT - 1, DIM * _r + CF * DENSE_SLOT, PAIRS + CF * _r, CF))
MLP_LOADS = len(W1_LOADS) + 4

COPY_FIRST = [0, 3, 6]

LAG = 2
TRANSPOSE_AFTER = [min(2, len(ks)) - 1 for ks in UNITS_OF_STEP]
MLP_PRODUCTS = H1 // P + H2 // P + 1
MLP_STEP = {0: [0, 1], 1: [2, 3], 2: [4, 5, 6]}
MLP_BEFORE = [0, 2, 4] + [MLP_PRODUCTS] * (CHUNKS - 3)


def dlrm_tower(nc, dense_ctx, ids, tables, W_top1, b_top1, W_top2, b_top2, W_top3, bil, out):
    with ExitStack() as ctx:
        def sb(name, shape, dt=F32):
            return ctx.enter_context(nc.sbuf_tensor(name, shape, dt))

        def ps(name, shape):
            return ctx.enter_context(nc.psum_tensor(name, shape, F32))

        def sem(name):
            return ctx.enter_context(nc.semaphore(name))

        idx = sb("idx", [P, 2, SUB, FIELDS // 2], I32)
        rows = sb("rows", [P, CHUNKS, SUB, CF, DIM])
        hilo = sb("hilo", [P, SUB, CF, 4, DIM], F32R)
        x_stack = sb("x_stack", [P, 2, CF, NB], F32R)
        x_T = sb("x_T", [P, CHUNKS, NB])
        W = sb("W", [P, W_COLS], F32R)
        W_signed_hi = sb("W_signed_hi", [P, 2, PIECE], F32R)
        prod = sb("prod", [P, P_SLOTS, CF, NB])
        z = sb("z", [P, ZT, NB])
        W1 = sb("W1", [P, ZT, H1])
        W2 = sb("W2", [P, H1 // P, H2])
        W3 = sb("W3", [P, H2 // P])
        b1 = sb("b1", [P, H1 // P])
        b2 = sb("b2", [P, H2 // P])
        h1 = sb("h1", [P, H1 // P, NB])
        h2 = sb("h2", [P, H2 // P, NB])
        y = sb("y", [1, NB])
        dense = sb("dense", [P, SUB, CF, DIM])
        ident = sb("ident", [P, P])
        select = sb("select", [P, 2 * DIM - CF])
        w_keep = sb("w_keep", [P, 1])
        w_sign = sb("w_sign", [P, 1])

        W_copy = nc.dram_tensor("W_copy", (PAIRS, DIM, DIM), F32).ap()

        U = ps("U", [P, U_SLOTS, CF, NB])
        bank_a = ps("bank_a", [P, 2, NB])
        bank_b = ps("bank_b", [P, 2, NB])
        bank_c = ps("bank_c", [P, 2, NB])
        bank_z = ps("bank_z", [P, 2, NB])

        ids_loaded = [sem("ids_loaded_early"), sem("ids_loaded_late")]
        zeroed, constants = sem("zeroed"), sem("constants")
        ident_made = sem("ident_made")
        gathered = [sem(f"gathered{c}") for c in range(CHUNKS)]
        hi_made, lo_made, hilo_made = sem("hi_made"), sem("lo_made"), sem("hilo_made")
        a_full, b_full, c_full = sem("a_full"), sem("b_full"), sem("c_full")
        a_kept, b_kept, c_kept = sem("a_kept"), sem("b_kept"), sem("c_kept")
        W_copied = [sem(f"W_copied{n}") for n in range(len(COPY_FIRST))]
        W_raw = [sem(f"W_raw{c}") for c in range(CHUNKS)]
        W_spread = [sem(f"W_spread{c}") for c in range(CHUNKS)]
        W_hi_made, W_split = sem("W_hi_made"), sem("W_split")
        mlp_loaded = sem("mlp_loaded")
        U_made, multiplied, summed = sem("U_made"), sem("multiplied"), sem("summed")
        z_kept = sem("z_kept")
        mlp_full, mlp_kept = sem("mlp_full"), sem("mlp_kept")
        y_stored = sem("y_stored")
        dense_loaded = sem("dense_loaded")
        pool_passed, sp_passed = sem("pool_passed"), sem("sp_passed")

        block = ctx.enter_context(nc.Block())

        def blocks(eng, one_block):
            one_block(0)
            with eng.Fori(1, BLOCKS - 1) as o:
                one_block(o)
            one_block(BLOCKS - 1)

        def first(o):
            return isinstance(o, int) and o == 0

        def next_chunk(o, c):
            if isinstance(o, int) and o == BLOCKS - 1 and c == CHUNKS - 1:
                return None
            return (c + 1) % CHUNKS, o * CHUNKS + c + 1

        def units_through(c):
            return UNITS_OF_STEP[c][-1] + 1

        def mlp_uses(o, c):
            return 0 if first(o) else (o - 1) * MLP_PRODUCTS + MLP_BEFORE[c]

        @block.sync
        def _(sp):
            def load_ids(o, half):
                f0 = (1 - half) * (FIELDS // 2)
                sp.dma_start(idx[:, half], ids[bass.ds(o * NB, NB), f0:f0 + FIELDS // 2].rearrange(
                    "(t p) f -> p t f", p=P)).then_inc(ids_loaded[half], 16)

            load_ids(0, 0)
            load_ids(0, 1)

            def copy_W(part):
                ends = [CF * (CHUNK_OF_STEP[c] + 1) for c in COPY_FIRST] + [0]
                lo, hi = pair(ends[part + 1], ends[part + 1] + 1), min(PAIRS, pair(ends[part], ends[part] + 1))
                sp.dma_start(W_copy[lo:hi], bil[lo:hi]).then_inc(W_copied[part], 16)

            def load_W(c):
                if c in COPY_FIRST:
                    sp.wait_ge(W_copied[COPY_FIRST.index(c)], 16)
                for i in range(CF * CHUNK_OF_STEP[c], CF * CHUNK_OF_STEP[c] + CF):
                    n = FIELDS - 1 - i
                    if n:
                        at = W_AT[i] + (i + 1 - W_J0[i]) * DIM
                        sp.dma_start(W[0:DIM, at:at + n * DIM].bitcast(F32).rearrange("d (j e) -> d j e", e=DIM),
                                     W_copy[pair(i, i + 1):pair(i, i + 1) + n].rearrange("j d e -> d j e")
                                     ).then_inc(W_raw[c], 16)

            def spread_W(c):
                sp.wait_ge(W_raw[c], 16 * (CF if c else CF - 1))
                lo, hi = W_REGION[c]
                for g in range(1, 4):
                    sp.dma_start(W[g * DIM:(g + 1) * DIM, lo:hi].bitcast(F32),
                                 W[0:DIM, lo:hi].bitcast(F32)).then_inc(W_spread[c], 16)

            def load_dense(o):
                for t in range(SUB):
                    sp.dma_start(dense[:, t, :, CF * DENSE_SLOT:],
                                 dense_ctx[bass.ds(o * NB + t * P, P), :].rearrange("p (r s) -> p r s", s=CF)
                                 ).then_inc(dense_loaded, 16)

            for part in range(len(COPY_FIRST)):
                copy_W(part)
            load_W(0)
            load_W(1)
            sp.wait_ge(zeroed, 1)
            for c in range(CHUNKS):
                spread_W(c)
                if c + 2 < CHUNKS:
                    load_W(c + 2)
                if c == 0:
                    load_dense(0)

            for t, row, at, n in W1_LOADS:
                sp.dma_start(W1[row:row + n, t, :], W_top1[at:at + n, :]).then_inc(mlp_loaded, 16)
            sp.dma_start(W2[:], W_top2.rearrange("(m p) n -> p m n", p=P)).then_inc(mlp_loaded, 16)
            with nc.allow_non_contiguous_dma(reason="biases and output column, a few values"):
                sp.dma_start(W3[:], W_top3.rearrange("(m p) o -> p (m o)", p=P)).then_inc(mlp_loaded, 16)
                sp.dma_start(b1[:], b_top1.rearrange("(m p) -> p m", p=P)).then_inc(mlp_loaded, 16)
                sp.dma_start(b2[:], b_top2.rearrange("(m p) -> p m", p=P)).then_inc(mlp_loaded, 16)

            def settle(sp):
                sp.sem_inc(sp_passed, 1)

            def store_y(o):
                sp.wait_ge(mlp_kept, o * MLP_PRODUCTS + MLP_PRODUCTS)
                settle(sp)
                sp.dma_start(out[bass.ds(o * NB, NB), :].rearrange("n o -> o n"), y[0:1, :]).then_inc(y_stored, 16)

            with sp.Fori(1, BLOCKS) as o:
                for half, c in ((0, CHUNKS // 2 - 1), (1, CHUNKS - 1)):
                    sp.wait_ge(gathered[c], o * (16 * SUB * CF))
                    settle(sp)
                    load_ids(o, half)
                sp.wait_ge(summed, o * NU)
                settle(sp)
                load_dense(o)
                store_y(o - 1)
            store_y(BLOCKS - 1)
            sp.wait_ge(y_stored, 16 * BLOCKS)

        @block.gpsimd
        def _(pool):
            nc.gpsimd.memset(ident[:], 0.0).then_inc(ident_made, 1)
            pool.wait_ge(ident_made, 1)
            nc.gpsimd.affine_select(out=ident[:], in_=ident[:], compare_op=ALU.not_equal, fill=1.0, base=0,
                                    pattern=[[-1, P]], channel_multiplier=1).then_inc(ident_made, 1)

            def gather_block(o):
                for c in range(CHUNKS):
                    if not first(o):
                        pool.wait_ge(c_full, (o - 1) * CHUNKS + c + 1)
                    if c % (CHUNKS // 2) == 0:
                        pool.wait_ge(ids_loaded[c // (CHUNKS // 2)], o * 16 + 16)
                    pool.sem_inc(pool_passed, 1)
                    half = c // (CHUNKS // 2)
                    for f in range(CF):
                        field = CF * CHUNK_OF_STEP[c] + f
                        for t in range(SUB):
                            nc.gpsimd.indirect_dma_start(
                                out=rows[:, c, t, f, :], out_offset=None, in_=tables[field][:, :],
                                in_offset=bass.IndirectOffsetOnAxis(
                                    ap=idx[:, half, t, field % (FIELDS // 2):field % (FIELDS // 2) + 1], axis=0),
                            ).then_inc(gathered[c], 16)

            gather_block(0)
            with pool.Fori(1, BLOCKS) as o:
                gather_block(o)

        @block.scalar
        def _(act):
            hilo_tf = hilo[:].rearrange("p t f g d -> p (t f) g d")

            def split_hi(o, c, n):
                act.wait_ge(gathered[c], o * (16 * SUB * CF) + 16 * SUB * CF)
                if not (first(o) and c == 0):
                    act.wait_ge(c_full, n)
                r = rows[:, c].rearrange("p t f d -> p (t f) d").unsqueeze(2).to_broadcast([P, SUB * CF, 2, DIM])
                nc.scalar.activation(hilo_tf[:, :, 0:2, :], r, ACT.Copy).then_inc(hi_made, 1)
                act.wait_ge(lo_made, n + 1)
                nc.scalar.activation(hilo_tf[:, :, 3, :], hilo_tf[:, :, 2, :].bitcast(F32), ACT.Copy
                                     ).then_inc(hilo_made, 1)

            def keep_chunk(o, c, n):
                if not (first(o) and c < 2):
                    act.wait_ge(U_made, (o * NU + units_through(c - 2)) if c >= 2 else
                                (o - 1) * NU + units_through(CHUNKS + c - 2))
                act.wait_ge(a_full, n + 1)
                nc.scalar.activation(x_stack[:, c % 2, 0:2, :], bank_a[:], ACT.Copy).then_inc(a_kept, 1)
                act.wait_ge(b_full, n + 1)
                nc.scalar.activation(x_stack[:, c % 2, 2:4, :], bank_b[:], ACT.Copy).then_inc(b_kept, 1)
                act.wait_ge(c_full, n + 1)
                if not first(o):
                    act.wait_ge(multiplied, (o - 1) * NU + UNITS.index((0, CHUNK_OF_STEP[c])) + 1)
                nc.scalar.activation(x_T[:, CHUNK_OF_STEP[c], :], bank_c[:, 0, :], ACT.Copy).then_inc(c_kept, 1)

            def split_W(c):
                act.wait_ge(W_spread[c], 48)
                for q, lo, hi in W_PIECES[c]:
                    if q >= 2:
                        act.wait_ge(W_split, q - 1)
                    nc.scalar.activation(W_signed_hi[:, q % 2, 0:hi - lo], W[:, lo:hi].bitcast(F32),
                                         ACT.Identity, scale=w_sign[:, 0:1]).then_inc(W_hi_made, 1)

            def keep_z(o, t):
                act.wait_ge(summed, o * NU + min(NU, t * UPT + UPT))
                if t == 0 and not first(o):
                    act.wait_ge(mlp_full, (o - 1) * MLP_PRODUCTS + H1 // P)
                nc.scalar.activation(z[:, t, :], bank_z[:, 0, :], ACT.Copy).then_inc(z_kept, 1)

            def mlp(o, c):
                act.wait_ge(mlp_loaded, 16 * MLP_LOADS)
                for j in MLP_STEP[c]:
                    bank = (bank_a, bank_b)[j % 2]
                    act.wait_ge(mlp_full, o * MLP_PRODUCTS + j + 1)
                    if j < H1 // P:
                        done = nc.scalar.activation(h1[:, j, :], bank[:, 0, :], ACT.Relu, bias=b1[:, j:j + 1])
                    elif j < MLP_PRODUCTS - 1:
                        m = j - H1 // P
                        done = nc.scalar.activation(h2[:, m, :], bank[:, 0, :], ACT.Relu, bias=b2[:, m:m + 1])
                    else:
                        if not first(o):
                            act.wait_ge(y_stored, o * 16)
                        done = nc.scalar.activation(y[0:1, :], bank_c[0:1, 0, :], ACT.Copy)
                    done.then_inc(mlp_kept, 1)

            def one_block(o):
                for c in range(CHUNKS):
                    nxt = next_chunk(o, c)
                    no = o if c + 1 < CHUNKS else o + 1
                    if nxt:
                        split_hi(no, *nxt)
                    if first(o):
                        split_W(c)
                    for u, k in enumerate(UNITS_OF_STEP[c]):
                        if k >= LAG and (k - LAG) % UPT == UPT - 1:
                            keep_z(o, (k - LAG) // UPT)
                        if nxt and u == TRANSPOSE_AFTER[c]:
                            keep_chunk(no, *nxt)
                    if c == CHUNKS - 1:
                        keep_z(o, ZT - 1)
                    if c in MLP_STEP and not first(o):
                        mlp(o - 1, c)

            act.wait_ge(constants, 1)
            split_hi(0, 0, 0)
            keep_chunk(0, 0, 0)
            blocks(act, one_block)
            for c in MLP_STEP:
                mlp(BLOCKS - 1, c)

        @block.vector
        def _(dve):
            nc.vector.memset(w_keep[:], 0.0)
            nc.vector.memset(w_sign[:], 1.0)
            for i in range(FIELDS):
                if W_J0[i] <= i:
                    nc.vector.memset(W[0:DIM, W_AT[i]:W_AT[i] + (i + 1 - W_J0[i]) * DIM].bitcast(F32), 0.0)
            nc.vector.memset(select[:], 0.0)
            nc.vector.memset(dense[:], 0.0)
            nc.vector.memset(W1[:], 0.0).then_inc(zeroed, 1)
            dve.wait_ge(zeroed, 1)
            for g in (1, 3):
                nc.vector.memset(w_keep[g * DIM:(g + 1) * DIM, :], 1.0)
                nc.vector.memset(w_sign[g * DIM:(g + 1) * DIM, :], -1.0)
            for s in range(CF):
                at = CF * (UPT - 1) + s
                last = nc.vector.memset(select[s * DIM:(s + 1) * DIM, at:at + 1], 1.0)
            last.then_inc(constants, 1)
            dve.wait_ge(constants, 1)

            def split_lo(n):
                c = n[0]
                dve.wait_ge(hi_made, n[1] + 1)
                hilo_tf = hilo[:].rearrange("p t f g d -> p (t f) g d")
                nc.vector.tensor_tensor(hilo_tf[:, :, 2, :], rows[:, c].rearrange("p t f d -> p (t f) d"),
                                        hilo_tf[:, :, 0, :].bitcast(F32), ALU.subtract).then_inc(lo_made, 1)

            def split_W(c):
                for q, lo, hi in W_PIECES[c]:
                    dve.wait_ge(W_hi_made, q + 1)
                    nc.vector.scalar_tensor_tensor(out=W[:, lo:hi], in0=W[:, lo:hi].bitcast(F32),
                                                   scalar=w_keep[:, 0:1],
                                                   in1=W_signed_hi[:, q % 2, 0:hi - lo].bitcast(F32),
                                                   op0=ALU.mult, op1=ALU.add).then_inc(W_split, 1)

            def multiply(o, c, k):
                a, J = UNITS[k]
                R = len(rows_of(k))
                g = o * NU + k
                if J == a:
                    dve.wait_ge(c_kept, o * CHUNKS + c + 1)
                dve.wait_ge(U_made, g + 1)
                if not (first(o) and k < P_SLOTS):
                    dve.wait_ge(summed, g - before(k, P_SLOTS) + 1)
                nc.vector.tensor_tensor(prod[:, k % P_SLOTS, 0:R, :], U[:, k % U_SLOTS, 0:R, :],
                                        x_T[:, J, :].unsqueeze(1).to_broadcast([P, R, NB]),
                                        ALU.mult).then_inc(multiplied, 1)

            def one_block(o):
                for c in range(CHUNKS):
                    nxt = next_chunk(o, c)
                    if nxt:
                        split_lo(nxt)
                    if first(o):
                        split_W(c)
                    for k in UNITS_OF_STEP[c]:
                        multiply(o, c, k)

            split_lo((0, 0))
            blocks(dve, one_block)

        @block.tensor
        def _(pe):
            def transpose_chunk(o, c, n, mlp_before):
                pe.wait_ge(hilo_made, n + 1)
                if not (isinstance(mlp_before, int) and mlp_before == 0):
                    pe.wait_ge(mlp_kept, mlp_before)
                started = not (first(o) and c == 0)
                for bank, full, kept, f0 in ((bank_a, a_full, a_kept, 0), (bank_b, b_full, b_kept, 2)):
                    if started:
                        pe.wait_ge(kept, n)
                    for f in range(2):
                        for t in range(SUB):
                            last = nc.tensor.transpose(
                                bank[:, f, t * P:(t + 1) * P],
                                hilo[:, t, f0 + f].bitcast(F32).rearrange("p g d -> p (g d)"), ident[:])
                    last.then_inc(full, 1)
                if started:
                    pe.wait_ge(c_kept, n)
                for t in range(SUB):
                    last = nc.tensor.transpose(bank_c[:, 0, t * P:(t + 1) * P],
                                               rows[:, c, t].rearrange("p f d -> p (f d)"), ident[:])
                last.then_inc(c_full, 1)

            def project(o, c, k):
                a, J = UNITS[k]
                if k == UNITS_OF_STEP[c][0]:
                    pe.wait_ge(b_kept, o * CHUNKS + c + 1)
                    if first(o):
                        pe.wait_ge(W_split, W_PIECES[c][-1][0] + 1)
                if not (first(o) and k < U_SLOTS):
                    pe.wait_ge(multiplied, o * NU + k - before(k, U_SLOTS) + 1)
                for r in rows_of(k):
                    at = W_AT[CF * a + r] + (CF * J - W_J0[CF * a + r]) * DIM
                    last = nc.tensor.matmul(U[:, k % U_SLOTS, r, :], W[:, at:at + P], x_stack[:, c % 2, r, :],
                                            start=True, stop=True, skip_group_check=True)
                last.then_inc(U_made, 1)

            def sum_up(o, k):
                t = k // UPT
                ks = [q for q in range(t * UPT, min(NU, t * UPT + UPT))]
                if k % UPT == 0 and not (first(o) and k == 0):
                    pe.wait_ge(z_kept, o * ZT + t)
                pe.wait_ge(multiplied, o * NU + k + 1)
                slot = SLOT[UNITS[k]]
                sel = select[:, CF * (UPT - 1 - slot):CF * (UPT - 1 - slot) + DIM]
                for r in rows_of(k):
                    users = [q for q in ks if r in rows_of(q)]
                    last = nc.tensor.matmul(bank_z[r * DIM:(r + 1) * DIM, 0, :], sel, prod[:, k % P_SLOTS, r, :],
                                            start=(k == users[0]), stop=(k == users[-1] and t < ZT - 1),
                                            skip_group_check=True)
                if k == NU - 1:
                    pe.wait_ge(dense_loaded, o * (16 * SUB) + 16 * SUB)
                    for r in range(CF):
                        for h in range(SUB):
                            last = nc.tensor.matmul(bank_z[r * DIM:(r + 1) * DIM, 0, h * P:(h + 1) * P],
                                                    dense[:, h, r, :], ident[:], start=False, stop=True,
                                                    skip_group_check=True)
                last.then_inc(summed, 1)

            def mlp(o, c, chunks):
                pe.wait_ge(mlp_loaded, 16 * MLP_LOADS)
                for j in MLP_STEP[c]:
                    if j == 0:
                        pe.wait_ge(z_kept, o * ZT + ZT)
                    bank, kept = ((bank_a, a_kept), (bank_b, b_kept))[j % 2]
                    if j < H1 // P:
                        m, tiles, w, x, res = j, ZT, W1, z, bank[:, 0, :]
                    elif j < MLP_PRODUCTS - 1:
                        m, tiles, w, x, res = j - H1 // P, H1 // P, W2, h1, bank[:, 0, :]
                    else:
                        m, tiles, w, x, res = 0, H2 // P, W3, h2, bank_c[0:1, 0, :]
                        kept = c_kept
                    pe.wait_ge(kept, chunks)
                    if j in (H1 // P, MLP_PRODUCTS - 1):
                        pe.wait_ge(mlp_kept, o * MLP_PRODUCTS + j)
                    elif j >= 2:
                        pe.wait_ge(mlp_kept, o * MLP_PRODUCTS + j - 1)
                    for t in range(tiles):
                        lhsT = w[:, t:t + 1] if w is W3 else w[:, t, m * P:(m + 1) * P]
                        last = nc.tensor.matmul(res, lhsT, x[:, t, :], start=(t == 0), stop=(t == tiles - 1))
                    last.then_inc(mlp_full, 1)

            def one_block(o):
                for c in range(CHUNKS):
                    nxt = next_chunk(o, c)
                    no = o if c + 1 < CHUNKS else o + 1
                    for u, k in enumerate(UNITS_OF_STEP[c]):
                        project(o, c, k)
                        if k >= LAG:
                            sum_up(o, k - LAG)
                        if nxt and u == TRANSPOSE_AFTER[c]:
                            transpose_chunk(no, *nxt, mlp_uses(o, c))
                    if c == CHUNKS - 1:
                        for k in range(NU - LAG, NU):
                            sum_up(o, k)
                    if c in MLP_STEP and not first(o):
                        mlp(o - 1, c, o * CHUNKS + c + 2)

            pe.wait_ge(ident_made, 2)
            pe.wait_ge(constants, 1)
            transpose_chunk(0, 0, 0, 0)
            blocks(pe, one_block)
            for c in MLP_STEP:
                mlp(BLOCKS - 1, c, BLOCKS * CHUNKS)


def kernel(**inputs):
    import concourse.bacc as bacc
    from concourse.bass_utils import run_bass_kernel_spmd

    nc = bacc.Bacc("TRN2", target_bir_lowering=False, num_devices=1)
    arrays, args = {}, {}
    for name, value in inputs.items():
        a = np.ascontiguousarray(value)
        arrays["in_" + name] = a
        args[name] = nc.dram_tensor("in_" + name, a.shape, mybir.dt.from_np(a.dtype), kind="ExternalInput").ap()
    out = nc.dram_tensor("out_y", (BATCH, 1), F32, kind="ExternalOutput").ap()
    dlrm_tower(nc, args["dense_ctx"], args["ids"], [args[f"tbl_{f}"] for f in range(FIELDS)], args["W_top1"],
               args["b_top1"], args["W_top2"], args["b_top2"], args["W_top3"], args["L0_rec_bilinear_matrices"], out)
    r = run_bass_kernel_spmd(nc, [arrays], core_ids=[0])
    return r.results[0]["out_y"]
```

```python
import numpy as np
import concourse.bass as bass
import concourse.mybir as mybir
from contextlib import ExitStack

F32 = mybir.dt.float32
F32R = mybir.dt.float32r
I32 = mybir.dt.int32
ALU = mybir.AluOpType
ACT = mybir.ActivationFunctionType

P = 128
FIELDS, DIM = 40, 32
BATCH, DENSE = 2048, 16
H1, H2 = 512, 256
NB = 256
BLOCKS = BATCH // NB
SUB = NB // P
CF = P // DIM
CHUNKS = FIELDS // CF
PAIRS = FIELDS * (FIELDS - 1) // 2

CHUNK_OF_STEP = [CHUNKS - 1 - c for c in range(CHUNKS)]
UNITS = [(a, J) for a in CHUNK_OF_STEP for J in range(CHUNKS - 1, a - 1, -1)]
NU = len(UNITS)
FIRST_UNIT = [UNITS.index((a, CHUNKS - 1)) for a in CHUNK_OF_STEP]
UNITS_OF_STEP = [[k for k in range(NU) if UNITS[k][0] == a] for a in CHUNK_OF_STEP]

UPT = 8
ZT = (NU + UPT - 1) // UPT
DENSE_SLOT = UPT - 1
assert NU % UPT == UPT - 1 and DENSE == CF * CF


def slot_runs():
    runs = []
    for t in range(ZT):
        ks = range(t * UPT, min(NU, (t + 1) * UPT))
        for a in CHUNK_OF_STEP:
            js = [UNITS[k][1] for k in ks if UNITS[k][0] == a]
            if js:
                first = min(k for k in ks if UNITS[k][0] == a) - t * UPT
                runs.append((t, a, min(js), max(js), first))
    return runs


RUNS = slot_runs()
SLOT = {(a, J): slot + J - lo for _, a, lo, hi, slot in RUNS for J in range(lo, hi + 1)}

GATHERS = 16 * SUB * CF
U_SLOTS, P_SLOTS = 2, 3
W_AHEAD = 3
PAIR = 2


def rows_of(k):
    a, J = UNITS[k]
    return range(CF - 1) if a == J else range(CF)


def pair(i, j):
    return i * (FIELDS - 1) - i * (i - 1) // 2 + (j - i - 1)


def ring_slot(b, k, slots):
    return (b * NU + k) % slots


def before(b, k, slots):
    at, n = b * NU + k, 1
    while (at - n) % (PAIR * NU) % slots != at % slots:
        n += 1
    return n


W_WIDTH = [P * (CHUNKS - a) for a in CHUNK_OF_STEP]
W_START = [sum(CF * w for w in W_WIDTH[:c]) for c in range(CHUNKS)]
W_COLS = W_START[-1] + CF * W_WIDTH[-1]


W1_LOADS = []
for _t, _a, _lo, _hi, _slot in RUNS:
    for _i in range(CF * _a, CF * _a + CF):
        _j = max(CF * _lo, _i + 1)
        if _j < CF * _hi + CF:
            W1_LOADS.append((_t, DIM * (_i - CF * _a) + CF * _slot + _j - CF * _lo, pair(_i, _j), CF * _hi + CF - _j))
for _r in range(CF):
    W1_LOADS.append((ZT - 1, DIM * _r + CF * DENSE_SLOT, PAIRS + CF * _r, CF))
MLP_LOADS = len(W1_LOADS) + 4

LAG = 2
PARTS_AFTER = [[min(u, len(ks) - 1) for u in (0, 1, 2)] for ks in UNITS_OF_STEP]
MLP_DEPTH = [ZT] * (H1 // P) + [H1 // P] * (H2 // P) + [H2 // P]
MLP_RESULTS = len(MLP_DEPTH)
MLP_JOBS = [(j, t) for j, depth in enumerate(MLP_DEPTH) for t in range(depth)]
MLP_AFTER = [[job for q, job in enumerate(MLP_JOBS) if q * NU // len(MLP_JOBS) == k] for k in range(NU)]
DENSE_AFTER = 5


def dlrm_tower(nc, dense_ctx, ids, tables, W_top1, b_top1, W_top2, b_top2, W_top3, bil, out):
    with ExitStack() as ctx:
        def sb(name, shape, dt=F32):
            return ctx.enter_context(nc.sbuf_tensor(name, shape, dt))

        def ps(name, shape):
            return ctx.enter_context(nc.psum_tensor(name, shape, F32))

        def sem(name):
            return ctx.enter_context(nc.semaphore(name))

        idx = sb("idx", [P, PAIR, SUB, FIELDS], I32)
        rows = sb("rows", [P, CHUNKS, SUB, CF, DIM])
        hilo = sb("hilo", [P, 2, SUB, CF, 4, DIM], F32R)
        x_stack = sb("x_stack", [P, 2, CF, NB], F32R)
        x_T = sb("x_T", [P, CHUNKS, NB])
        W = sb("W", [P, W_COLS], F32R)
        W_parts = sb("W_parts", [P, 2, W_WIDTH[-1]], F32R)
        prod = sb("prod", [P, P_SLOTS, CF, NB])
        z = sb("z", [P, PAIR, ZT, NB])
        W1 = sb("W1", [P, ZT, H1])
        W_in = [W1[:].rearrange("p t n -> p (t n)")[:, h * W_WIDTH[-1]:(h + 1) * W_WIDTH[-1]] for h in range(2)]
        W2 = sb("W2", [P, H1 // P, H2])
        W3 = sb("W3", [P, H2 // P])
        b1 = sb("b1", [P, H1 // P])
        b2 = sb("b2", [P, H2 // P])
        h_cols = W_parts[:].bitcast(F32).rearrange("p s n -> p (s n)")
        h1 = h_cols[:, 0:H1 // P * NB].rearrange("p (m n) -> p m n", n=NB)
        h2 = h_cols[:, H1 // P * NB:(H1 + H2) // P * NB].rearrange("p (m n) -> p m n", n=NB)
        y = sb("y", [1, NB])
        dense = sb("dense", [P, SUB, CF, DIM])
        ident = sb("ident", [P, P])
        ident_r = sb("ident_r", [P, P], F32R)
        select = sb("select", [P, 2 * DIM - CF])

        W_hilo = [nc.dram_tensor(f"W_hilo{c}", (2, P, W_WIDTH[c]), F32).ap() for c in range(CHUNKS)]

        U = ps("U", [P, U_SLOTS, CF, NB])
        bank_a = ps("bank_a", [P, 2, NB])
        bank_b = ps("bank_b", [P, 2, NB])
        bank_mlp = ps("bank_mlp", [P, 2, NB])
        bank_z = ps("bank_z", [P, 2, NB])

        ids_loaded = [sem(f"ids_loaded{b}") for b in range(PAIR)]
        zeroed, constants = sem("zeroed"), sem("constants")
        ident_made, ident_r_made = sem("ident_made"), sem("ident_r_made")
        gathered = [sem(f"gathered{c}") for c in range(CHUNKS)]
        hi_made, lo_made, hilo_made = sem("hi_made"), sem("lo_made"), sem("hilo_made")
        a_full, b_full, c_full = sem("a_full"), sem("b_full"), sem("c_full")
        a_kept, b_kept, c_kept = sem("a_kept"), sem("b_kept"), sem("c_kept")
        W_in_landed = [sem(f"W_in_landed{c}") for c in range(CHUNKS)]
        W_hi_made, W_lo_made = sem("W_hi_made"), sem("W_lo_made")
        W_stored = [sem(f"W_stored{c}") for c in range(CHUNKS)]
        W_ready = [sem(f"W_ready{c}") for c in range(CHUNKS)]
        W1_zeroed = sem("W1_zeroed")
        mlp_loaded = sem("mlp_loaded")
        U_made, multiplied, summed = sem("U_made"), sem("multiplied"), sem("summed")
        z_kept = sem("z_kept")
        mlp_full, mlp_kept = sem("mlp_full"), sem("mlp_kept")
        y_stored = sem("y_stored")
        dense_loaded = sem("dense_loaded")
        pool_passed, sp_passed = sem("pool_passed"), sem("sp_passed")

        block = ctx.enter_context(nc.Block())

        def blocks(eng, one_block):
            one_block(0, 0)
            with eng.Fori(1, BLOCKS // PAIR) as turn:
                one_block(turn * PAIR - 1, 1)
                one_block(turn * PAIR, 0)
            one_block(BLOCKS - 1, 1)

        def first(o):
            return isinstance(o, int) and o == 0

        def ahead(by, o, c):
            if isinstance(o, int) and o * CHUNKS + c + by >= BLOCKS * CHUNKS:
                return None
            return (o if c + by < CHUNKS else o + 1), (c + by) % CHUNKS, o * CHUNKS + c + by

        def mlp_bank(j, closing):
            return (bank_mlp, bank_a, bank_b)[j % 3] if closing else bank_mlp

        def units_through(c):
            return UNITS_OF_STEP[c][-1] + 1

        @block.sync
        def _(sp):
            def load_ids(o, b):
                sp.dma_start(idx[:, b], ids[bass.ds(o * NB, NB), :].rearrange("(t p) f -> p t f", p=P)
                             ).then_inc(ids_loaded[b], 16)

            load_ids(0, 0)
            load_ids(1, 1)

            def load_W(c):
                for r in range(CF):
                    i = CF * CHUNK_OF_STEP[c] + r
                    if i < FIELDS - 1:
                        sp.dma_start(W_in[c % 2][r * DIM:(r + 1) * DIM, (r + 1) * DIM:W_WIDTH[c]].rearrange(
                                         "d (j e) -> d j e", e=DIM),
                                     bil[pair(i, i + 1):pair(i, FIELDS - 1) + 1].rearrange("j d e -> d j e")
                                     ).then_inc(W_in_landed[c], 16)

            sp.wait_ge(zeroed, 1)
            load_W(0)
            load_W(1)
            for c in range(CHUNKS):
                w = W_WIDTH[c]
                sp.wait_ge(W_lo_made, c + 1)
                for part in range(2):
                    sp.dma_start(W_hilo[c][part], W_parts[:, part, 0:w].bitcast(F32)).then_inc(W_stored[c], 16)
                if c + 2 < CHUNKS:
                    load_W(c + 2)
                sp.wait_ge(W_stored[c], 32)
                for g, part in enumerate((0, 1, 0, 1)):
                    sp.dma_start(W[g * DIM:(g + 1) * DIM, W_START[c]:W_START[c] + CF * w].bitcast(F32).rearrange(
                                     "d (r n) -> d r n", r=CF),
                                 W_hilo[c][part].rearrange("(r d) n -> d r n", r=CF)).then_inc(W_ready[c], 16)

            sp.wait_ge(W1_zeroed, 1)
            for t, row, at, n in W1_LOADS:
                sp.dma_start(W1[row:row + n, t, :], W_top1[at:at + n, :]).then_inc(mlp_loaded, 16)
            sp.dma_start(W2[:], W_top2.rearrange("(m p) n -> p m n", p=P)).then_inc(mlp_loaded, 16)
            with nc.allow_non_contiguous_dma(reason="biases and output column, a few values"):
                sp.dma_start(W3[:], W_top3.rearrange("(m p) o -> p (m o)", p=P)).then_inc(mlp_loaded, 16)
                sp.dma_start(b1[:], b_top1.rearrange("(m p) -> p m", p=P)).then_inc(mlp_loaded, 16)
                sp.dma_start(b2[:], b_top2.rearrange("(m p) -> p m", p=P)).then_inc(mlp_loaded, 16)

            with sp.Fori(1, BLOCKS // PAIR) as turn:
                for b in range(PAIR):
                    sp.wait_ge(gathered[CHUNKS - 1], turn * (PAIR * GATHERS) + (b - 1) * GATHERS)
                    sp.sem_inc(sp_passed, 1)
                    load_ids(turn * PAIR + b, b)

        @block.gpsimd
        def _(pool):
            nc.gpsimd.memset(ident[:], 0.0).then_inc(ident_made, 1)
            pool.wait_ge(ident_made, 1)
            nc.gpsimd.affine_select(out=ident[:], in_=ident[:], compare_op=ALU.not_equal, fill=1.0, base=0,
                                    pattern=[[-1, P]], channel_multiplier=1).then_inc(ident_made, 1)

            def gather_block(o, b, ids_count):
                for c in range(CHUNKS):
                    if not first(o):
                        pool.wait_ge(c_full, (o - 1) * CHUNKS + c + 1)
                    if c == 0:
                        pool.wait_ge(ids_loaded[b], ids_count)
                    pool.sem_inc(pool_passed, 1)
                    for f in range(CF):
                        field = CF * CHUNK_OF_STEP[c] + f
                        for t in range(SUB):
                            nc.gpsimd.indirect_dma_start(
                                out=rows[:, c, t, f, :], out_offset=None, in_=tables[field][:, :],
                                in_offset=bass.IndirectOffsetOnAxis(
                                    ap=idx[:, b, t, field:field + 1], axis=0),
                            ).then_inc(gathered[c], 16)

            for b in range(PAIR):
                gather_block(b, b, 16)
            with pool.Fori(1, BLOCKS // PAIR) as turn:
                for b in range(PAIR):
                    gather_block(turn * PAIR + b, b, turn * 16 + 16)

        @block.scalar
        def _(act):
            def split_hi(o, c, n):
                act.wait_ge(gathered[c], o * GATHERS + GATHERS)
                if not (first(o) and c < 2):
                    act.wait_ge(b_full, n - 1)
                h = hilo[:, c % 2].rearrange("p t f g d -> p (t f) g d")
                r = rows[:, c].rearrange("p t f d -> p (t f) d").unsqueeze(2).to_broadcast([P, SUB * CF, 2, DIM])
                nc.scalar.activation(h[:, :, 0:2, :], r, ACT.Copy).then_inc(hi_made, 1)

            def repeat_lo(o, c, n):
                h = hilo[:, c % 2].rearrange("p t f g d -> p (t f) g d")
                act.wait_ge(lo_made, n + 1)
                nc.scalar.activation(h[:, :, 3, :], h[:, :, 2, :].bitcast(F32), ACT.Copy).then_inc(hilo_made, 1)

            def keep_part(part, o, c, n):
                if part == 0:
                    if not (first(o) and c < 2):
                        act.wait_ge(U_made, (o * NU + units_through(c - 2)) if c >= 2 else
                                    (o * NU - NU + units_through(CHUNKS + c - 2)))
                    act.wait_ge(a_full, n + 1)
                    nc.scalar.activation(x_stack[:, c % 2, 0:2, :], bank_a[:], ACT.Copy).then_inc(a_kept, 1)
                elif part == 1:
                    act.wait_ge(b_full, n + 1)
                    nc.scalar.activation(x_stack[:, c % 2, 2:4, :], bank_b[:], ACT.Copy).then_inc(b_kept, 1)
                else:
                    act.wait_ge(c_full, n + 1)
                    if not first(o):
                        act.wait_ge(multiplied, o * NU - NU + UNITS.index((0, CHUNK_OF_STEP[c])) + 1)
                    nc.scalar.activation(x_T[:, CHUNK_OF_STEP[c], :], bank_a[:, 0, :], ACT.Copy).then_inc(c_kept, 1)

            def split_W(c):
                act.wait_ge(W_in_landed[c], 16 * (CF if c else CF - 1))
                if c:
                    act.wait_ge(W_stored[c - 1], 32)
                nc.scalar.activation(W_parts[:, 0, 0:W_WIDTH[c]], W_in[c % 2][:, 0:W_WIDTH[c]], ACT.Copy
                                     ).then_inc(W_hi_made, 1)

            def keep_z(o, b, t):
                act.wait_ge(summed, o * NU + min(NU, t * UPT + UPT))
                nc.scalar.activation(z[:, b, t, :], bank_z[:, 0, :], ACT.Copy).then_inc(z_kept, 1)

            def keep_mlp(o, j, closing=False):
                bank = mlp_bank(j, closing)
                act.wait_ge(mlp_full, o * MLP_RESULTS + j + 1)
                if j == 0:
                    act.wait_ge(W_stored[CHUNKS - 1], 32)
                if j < H1 // P:
                    done = nc.scalar.activation(h1[:, j, :], bank[:, 0, :], ACT.Relu, bias=b1[:, j:j + 1])
                elif j < MLP_RESULTS - 1:
                    m = j - H1 // P
                    done = nc.scalar.activation(h2[:, m, :], bank[:, 0, :], ACT.Relu, bias=b2[:, m:m + 1])
                else:
                    if not first(o):
                        act.wait_ge(y_stored, o * 16)
                    done = nc.scalar.activation(y[0:1, :], bank[0:1, 0, :], ACT.Copy)
                done.then_inc(mlp_kept, 1)
                if j == MLP_RESULTS - 1:
                    act.wait_ge(mlp_kept, o * MLP_RESULTS + MLP_RESULTS)
                    act.dma_start(out[bass.ds(o * NB, NB), :].rearrange("n o -> o n"), y[0:1, :]
                                  ).then_inc(y_stored, 16)

            def load_dense(o):
                for t in range(SUB):
                    act.dma_start(dense[:, t, :, CF * DENSE_SLOT:],
                                  dense_ctx[bass.ds(o * NB + t * P, P), :].rearrange("p (r s) -> p r s", s=CF)
                                  ).then_inc(dense_loaded, 16)

            def one_block(o, b):
                for c in range(CHUNKS):
                    nxt, split = ahead(1, o, c), ahead(2, o, c)
                    if first(o) and c + W_AHEAD < CHUNKS:
                        split_W(c + W_AHEAD)
                    if split:
                        split_hi(*split)
                    for u, k in enumerate(UNITS_OF_STEP[c]):
                        if k >= LAG and (k - LAG) % UPT == UPT - 1:
                            keep_z(o, b, (k - LAG) // UPT)
                        for part, after in enumerate(PARTS_AFTER[c]):
                            if nxt and u == after:
                                keep_part(part, *nxt)
                        if split and u == 0:
                            repeat_lo(*split)
                        if not first(o):
                            for j, t in MLP_AFTER[k]:
                                if t == MLP_DEPTH[j] - 1:
                                    keep_mlp(o - 1, j)
                            if k == DENSE_AFTER:
                                load_dense(o)
                keep_z(o, b, ZT - 1)

            act.wait_ge(ident_made, 2)
            nc.scalar.activation(ident_r[:], ident[:], ACT.Copy).then_inc(ident_r_made, 1)
            act.wait_ge(zeroed, 1)
            load_dense(0)
            for c in range(W_AHEAD):
                split_W(c)
            for c in range(2):
                split_hi(0, c, c)
                repeat_lo(0, c, c)
                if c == 0:
                    for part in range(3):
                        keep_part(part, 0, 0, 0)
            blocks(act, one_block)
            for j in range(MLP_RESULTS):
                keep_mlp(BLOCKS - 1, j, closing=True)
            act.wait_ge(y_stored, 16 * BLOCKS)

        @block.vector
        def _(dve):
            for half in W_in:
                nc.vector.memset(half[:, 0:P], 0.0)
            nc.vector.memset(select[:], 0.0)
            nc.vector.memset(dense[:], 0.0).then_inc(zeroed, 1)
            dve.wait_ge(zeroed, 1)
            for s in range(CF):
                at = CF * (UPT - 1) + s
                last = nc.vector.memset(select[s * DIM:(s + 1) * DIM, at:at + 1], 1.0)
            last.then_inc(constants, 1)

            def split_lo(o, c, n):
                dve.wait_ge(hi_made, n + 1)
                h = hilo[:, c % 2].rearrange("p t f g d -> p (t f) g d")
                nc.vector.tensor_tensor(h[:, :, 2, :], rows[:, c].rearrange("p t f d -> p (t f) d"),
                                        h[:, :, 0, :].bitcast(F32), ALU.subtract).then_inc(lo_made, 1)

            def split_W(c):
                dve.wait_ge(W_hi_made, c + 1)
                nc.vector.tensor_tensor(W_parts[:, 1, 0:W_WIDTH[c]], W_in[c % 2][:, 0:W_WIDTH[c]],
                                        W_parts[:, 0, 0:W_WIDTH[c]].bitcast(F32), ALU.subtract
                                        ).then_inc(W_lo_made, 1)
                if c == CHUNKS - 1:
                    dve.wait_ge(W_lo_made, CHUNKS)
                    nc.vector.memset(W1[:], 0.0).then_inc(W1_zeroed, 1)

            def multiply(o, b, c, k):
                a, J = UNITS[k]
                R = len(rows_of(k))
                g = o * NU + k
                if J == a:
                    dve.wait_ge(c_kept, o * CHUNKS + c + 1)
                dve.wait_ge(U_made, g + 1)
                if not (first(o) and k < P_SLOTS):
                    dve.wait_ge(summed, g - before(b, k, P_SLOTS) + 1)
                nc.vector.tensor_tensor(prod[:, ring_slot(b, k, P_SLOTS), 0:R, :], U[:, ring_slot(b, k, U_SLOTS), 0:R, :],
                                        x_T[:, J, :].unsqueeze(1).to_broadcast([P, R, NB]),
                                        ALU.mult).then_inc(multiplied, 1)

            def one_block(o, b):
                for c in range(CHUNKS):
                    split = ahead(2, o, c)
                    if first(o) and c + W_AHEAD < CHUNKS:
                        split_W(c + W_AHEAD)
                    for u, k in enumerate(UNITS_OF_STEP[c]):
                        multiply(o, b, c, k)
                        if split and u == 0:
                            split_lo(*split)

            for c in range(W_AHEAD):
                split_W(c)
            for c in range(2):
                split_lo(0, c, c)
            blocks(dve, one_block)

        @block.tensor
        def _(pe):
            def transpose_part(part, o, c, n):
                started = not (first(o) and c == 0)
                if part == 0:
                    pe.wait_ge(hilo_made, n + 1)
                    if started:
                        pe.wait_ge(c_kept, n)
                elif part == 1 and started:
                    pe.wait_ge(b_kept, n)
                elif part == 2:
                    pe.wait_ge(a_kept, n + 1)
                for t in range(SUB):
                    if part < 2:
                        for f in range(2):
                            last = nc.tensor.matmul(
                                (bank_a, bank_b)[part][:, f, t * P:(t + 1) * P],
                                hilo[:, c % 2, t, 2 * part + f].rearrange("p g d -> p (g d)"), ident_r[:],
                                start=True, stop=True, skip_group_check=True)
                    else:
                        last = nc.tensor.transpose(bank_a[:, 0, t * P:(t + 1) * P],
                                                   rows[:, c, t].rearrange("p f d -> p (f d)"), ident[:])
                last.then_inc((a_full, b_full, c_full)[part], 1)

            def project(o, b, c, k):
                a, J = UNITS[k]
                if k == UNITS_OF_STEP[c][0]:
                    pe.wait_ge(b_kept, o * CHUNKS + c + 1)
                    if first(o):
                        pe.wait_ge(W_ready[c], 64)
                if not (first(o) and k < U_SLOTS):
                    pe.wait_ge(multiplied, o * NU + k - before(b, k, U_SLOTS) + 1)
                for r in rows_of(k):
                    at = W_START[c] + r * W_WIDTH[c] + (J - a) * P
                    last = nc.tensor.matmul(U[:, ring_slot(b, k, U_SLOTS), r, :], W[:, at:at + P],
                                            x_stack[:, c % 2, r, :], start=True, stop=True, skip_group_check=True)
                last.then_inc(U_made, 1)

            def sum_up(o, b, k):
                t = k // UPT
                if k % UPT == 0 and not (first(o) and k == 0):
                    pe.wait_ge(z_kept, o * ZT + t)
                pe.wait_ge(multiplied, o * NU + k + 1)
                slot = SLOT[UNITS[k]]
                sel = select[:, CF * (UPT - 1 - slot):CF * (UPT - 1 - slot) + DIM]
                for r in rows_of(k):
                    users = [q for q in range(t * UPT, min(NU, t * UPT + UPT)) if r in rows_of(q)]
                    last = nc.tensor.matmul(bank_z[r * DIM:(r + 1) * DIM, 0, :], sel,
                                            prod[:, ring_slot(b, k, P_SLOTS), r, :],
                                            start=(k == users[0]), stop=(k == users[-1] and t < ZT - 1),
                                            skip_group_check=True)
                if k == NU - 1:
                    pe.wait_ge(dense_loaded, o * (16 * SUB) + 16 * SUB)
                    for r in range(CF):
                        for h in range(SUB):
                            last = nc.tensor.matmul(bank_z[r * DIM:(r + 1) * DIM, 0, h * P:(h + 1) * P],
                                                    dense[:, h, r, :], ident[:], start=False, stop=True,
                                                    skip_group_check=True)
                last.then_inc(summed, 1)

            def mlp(o, b, j, t, closing=False):
                if j == 0 and t == 0:
                    pe.wait_ge(mlp_loaded, 16 * MLP_LOADS)
                if j == 0 and t == ZT - 1:
                    pe.wait_ge(z_kept, o * ZT + ZT)
                bank = mlp_bank(j, closing)
                if t == 0 and closing and j in (1, 2):
                    pe.wait_ge((c_kept, b_kept)[j - 1], BLOCKS * CHUNKS)
                elif t == 0 and closing and j == 3:
                    pe.wait_ge(mlp_kept, o * MLP_RESULTS + 1)
                elif t == 0 and closing and j == H1 // P + 1:
                    pass
                elif t == 0 and not (first(o) and j == 0):
                    pe.wait_ge(mlp_kept, o * MLP_RESULTS + j)
                if j < H1 // P:
                    last = nc.tensor.matmul(bank[:, 0, :], W1[:, t, j * P:(j + 1) * P], z[:, b, t, :],
                                            start=(t == 0), stop=(t == ZT - 1))
                elif j < MLP_RESULTS - 1:
                    m = j - H1 // P
                    last = nc.tensor.matmul(bank[:, 0, :], W2[:, t, m * P:(m + 1) * P], h1[:, t, :],
                                            start=(t == 0), stop=(t == MLP_DEPTH[j] - 1))
                else:
                    last = nc.tensor.matmul(bank[0:1, 0, :], W3[:, t:t + 1], h2[:, t, :],
                                            start=(t == 0), stop=(t == MLP_DEPTH[j] - 1))
                if t == MLP_DEPTH[j] - 1:
                    last.then_inc(mlp_full, 1)

            def one_block(o, b):
                for c in range(CHUNKS):
                    nxt = ahead(1, o, c)
                    for u, k in enumerate(UNITS_OF_STEP[c]):
                        project(o, b, c, k)
                        if k >= LAG:
                            sum_up(o, b, k - LAG)
                        for part, after in enumerate(PARTS_AFTER[c]):
                            if nxt and u == after:
                                transpose_part(part, *nxt)
                        if not first(o):
                            for j, t in MLP_AFTER[k]:
                                mlp(o - 1, 1 - b, j, t)
                for k in range(NU - LAG, NU):
                    sum_up(o, b, k)

            pe.wait_ge(ident_made, 2)
            pe.wait_ge(ident_r_made, 1)
            pe.wait_ge(constants, 1)
            for part in range(3):
                transpose_part(part, 0, 0, 0)
            blocks(pe, one_block)
            for j, t in MLP_JOBS:
                mlp(BLOCKS - 1, 1, j, t, closing=True)


def kernel(**inputs):
    import concourse.bacc as bacc
    from concourse.bass_utils import run_bass_kernel_spmd

    nc = bacc.Bacc("TRN2", target_bir_lowering=False, num_devices=1)
    arrays, args = {}, {}
    for name, value in inputs.items():
        a = np.ascontiguousarray(value)
        arrays["in_" + name] = a
        args[name] = nc.dram_tensor("in_" + name, a.shape, mybir.dt.from_np(a.dtype), kind="ExternalInput").ap()
    out = nc.dram_tensor("out_y", (BATCH, 1), F32, kind="ExternalOutput").ap()
    dlrm_tower(nc, args["dense_ctx"], args["ids"], [args[f"tbl_{f}"] for f in range(FIELDS)], args["W_top1"],
               args["b_top1"], args["W_top2"], args["b_top2"], args["W_top3"], args["L0_rec_bilinear_matrices"], out)
    r = run_bass_kernel_spmd(nc, [arrays], core_ids=[0])
    return r.results[0]["out_y"]
```
